# Optimizing a Trainium2 kernel written in Bass

```python
import numpy as np
import jax
import jax.numpy as jnp

def _softmax(x, axis=-1):
    return jax.nn.softmax(x, axis=axis)

def _gelu(x):
    return jax.nn.gelu(x, approximate=True)

def _silu(x):
    return jax.nn.silu(x)

def _sigmoid(x):
    return jax.nn.sigmoid(x)

def _layernorm(x, axis=-1, eps=1e-05):
    m = jnp.mean(x, axis=axis, keepdims=True)
    v = jnp.var(x, axis=axis, keepdims=True)
    return (x - m) / jnp.sqrt(v + eps)

def _scatter_add(tgt, idx, src, axis=0):
    return tgt.at[idx].add(src)

def _segment_sum(src, seg, n):
    return jax.ops.segment_sum(src, seg, n)
kernel_name = 'mk_seq_postln_d1_jaxref_r8_0d6e83'

def setup_inputs(seed: int=0):
    np.random.seed(seed)
    _w = jnp.asarray

    def _L0_attn_setup():
        import jax, jax.numpy as jnp
        import numpy as np
        N_HEAD = 16
        W_SCALE = 0.02

        def _mla_forward(x, Wdq, Wuq, Wdkv, Wuk, Wuv, Wo):
            B, T, C = x.shape
            nh = N_HEAD
            hs = C // nh
            Lkv = Wdkv.shape[0]
            k_eff = (Wdq.T @ Wuq.T @ Wuk).reshape(nh, hs, Lkv)
            v_eff = (Wuv.T @ Wo.T).reshape(Lkv, nh, hs).transpose(1, 0, 2)
            c_kv = x @ Wdkv.T
            q = (x @ Wdq.T @ Wuq.T).reshape(B, T, nh, hs).transpose(0, 2, 1, 3)
            q_lat = jnp.einsum('bhtd,hdl->bhtl', q, k_eff)
            scores = jnp.einsum('bhtl,bsl->bhts', q_lat, c_kv) / jnp.sqrt(jnp.float32(hs))
            causal = jnp.tril(jnp.ones((T, T), dtype=bool))
            scores = jnp.where(causal[None, None, :, :], scores, jnp.finfo(scores.dtype).min)
            attn = jax.nn.softmax(scores, axis=-1)
            ctx = jnp.einsum('bhts,bsl->bhtl', attn, c_kv)
            y = jnp.einsum('bhtl,hld->bhtd', ctx, v_eff)
            y = y.transpose(0, 2, 1, 3).reshape(B, T, C)
            return (y, c_kv)

        def _reference_tuple_inner(x, Wdq, Wuq, Wdkv, Wuk, Wuv, Wo):
            y, updated_kv_cache = _mla_forward(x, Wdq, Wuq, Wdkv, Wuk, Wuv, Wo)
            return (y, updated_kv_cache)
        key = jax.random.key(seed)
        ks = jax.random.split(key, 7)
        B, T, C, Lq, Lkv = (2, 256, 256, 64, 64)
        x = jax.random.normal(ks[0], (B, T, C), dtype=jnp.float32)
        Wdq = jax.random.normal(ks[1], (Lq, C), dtype=jnp.float32) * W_SCALE
        Wuq = jax.random.normal(ks[2], (C, Lq), dtype=jnp.float32) * W_SCALE
        Wdkv = jax.random.normal(ks[3], (Lkv, C), dtype=jnp.float32) * W_SCALE
        Wuk = jax.random.normal(ks[4], (C, Lkv), dtype=jnp.float32) * W_SCALE
        Wuv = jax.random.normal(ks[5], (C, Lkv), dtype=jnp.float32) * W_SCALE
        Wo = jax.random.normal(ks[6], (C, C), dtype=jnp.float32) * W_SCALE
        return {'x': x, 'Wdq': Wdq, 'Wuq': Wuq, 'Wdkv': Wdkv, 'Wuk': Wuk, 'Wuv': Wuv, 'Wo': Wo}
    _L0_attn_in = _L0_attn_setup()

    def _L0_ffn_setup():
        import jax, jax.numpy as jnp
        import numpy as np
        BLOCK_SIZE = 32
        FP4_GRID = jnp.array([0.0, 0.5, 1.0, 1.5, 2.0, 3.0, 4.0, 6.0], dtype=jnp.float32)
        FP4_MIDS = jnp.array([0.25, 0.75, 1.25, 1.75, 2.5, 3.5, 5.0], dtype=jnp.float32)

        def quantize_to_mxfp4(w, block_size=BLOCK_SIZE):
            K, N = w.shape
            wb = w.reshape(K // block_size, block_size, N)
            amax = jnp.max(jnp.abs(wb), axis=1, keepdims=True)
            exp = jnp.floor(jnp.log2(jnp.maximum(amax, 1e-30))) - 2.0
            scales = jnp.exp2(exp)
            x = wb / scales
            idx = jnp.digitize(jnp.abs(x), FP4_MIDS)
            q = jnp.sign(x) * FP4_GRID[idx]
            return (q, scales)

        def mxfp4_matmul(inputs, q, scales, block_size=BLOCK_SIZE):
            K = inputs.shape[-1]
            N = q.shape[-1]
            w = (q * scales).reshape(K, N)
            return inputs @ w
        key = jax.random.key(seed)
        ks = jax.random.split(key, 3)
        B, S, D, F = (4, 256, 256, 1024)
        inputs = jax.random.normal(ks[0], (B, S, D), dtype=jnp.float32)
        up_kernel = jax.random.normal(ks[1], (D, F), dtype=jnp.float32) * (1.0 / np.sqrt(D))
        down_kernel = jax.random.normal(ks[2], (F, D), dtype=jnp.float32) * (1.0 / np.sqrt(F))
        up_bias = jnp.zeros((F,), dtype=jnp.float32)
        down_bias = jnp.zeros((D,), dtype=jnp.float32)
        return {'inputs': inputs, 'up_kernel': up_kernel, 'up_bias': up_bias, 'down_kernel': down_kernel, 'down_bias': down_bias}
    _L0_ffn_in = _L0_ffn_setup()
    _d = {'L0_attn_x': _L0_attn_in['x'], 'L0_attn_Wdq': _L0_attn_in['Wdq'], 'L0_attn_Wuq': _L0_attn_in['Wuq'], 'L0_attn_Wdkv': _L0_attn_in['Wdkv'], 'L0_attn_Wuk': _L0_attn_in['Wuk'], 'L0_attn_Wuv': _L0_attn_in['Wuv'], 'L0_attn_Wo': _L0_attn_in['Wo'], 'L0_ffn_up_kernel': _L0_ffn_in['up_kernel'], 'L0_ffn_up_bias': _L0_ffn_in['up_bias'], 'L0_ffn_down_kernel': _L0_ffn_in['down_kernel'], 'L0_ffn_down_bias': _L0_ffn_in['down_bias']}
    _x0 = _d['L0_attn_x']
    _d['L0_attn_x'] = jax.random.normal(jax.random.fold_in(jax.random.key(seed), 1), (16, 256, 256), dtype=_x0.dtype)
    del _x0
    return _d

def reference(L0_attn_x, L0_attn_Wdq, L0_attn_Wuq, L0_attn_Wdkv, L0_attn_Wuk, L0_attn_Wuv, L0_attn_Wo, L0_ffn_up_kernel, L0_ffn_up_bias, L0_ffn_down_kernel, L0_ffn_down_bias):

    def _L0_attn_ref(x, Wdq, Wuq, Wdkv, Wuk, Wuv, Wo):
        import jax, jax.numpy as jnp
        import numpy as np
        N_HEAD = 16
        W_SCALE = 0.02

        def _mla_forward(x, Wdq, Wuq, Wdkv, Wuk, Wuv, Wo):
            B, T, C = x.shape
            nh = N_HEAD
            hs = C // nh
            Lkv = Wdkv.shape[0]
            k_eff = (Wdq.T @ Wuq.T @ Wuk).reshape(nh, hs, Lkv)
            v_eff = (Wuv.T @ Wo.T).reshape(Lkv, nh, hs).transpose(1, 0, 2)
            c_kv = x @ Wdkv.T
            q = (x @ Wdq.T @ Wuq.T).reshape(B, T, nh, hs).transpose(0, 2, 1, 3)
            q_lat = jnp.einsum('bhtd,hdl->bhtl', q, k_eff)
            scores = jnp.einsum('bhtl,bsl->bhts', q_lat, c_kv) / jnp.sqrt(jnp.float32(hs))
            causal = jnp.tril(jnp.ones((T, T), dtype=bool))
            scores = jnp.where(causal[None, None, :, :], scores, jnp.finfo(scores.dtype).min)
            attn = jax.nn.softmax(scores, axis=-1)
            ctx = jnp.einsum('bhts,bsl->bhtl', attn, c_kv)
            y = jnp.einsum('bhtl,hld->bhtd', ctx, v_eff)
            y = y.transpose(0, 2, 1, 3).reshape(B, T, C)
            return (y, c_kv)

        def _reference_tuple_inner(x, Wdq, Wuq, Wdkv, Wuk, Wuv, Wo):
            y, updated_kv_cache = _mla_forward(x, Wdq, Wuq, Wdkv, Wuk, Wuv, Wo)
            return (y, updated_kv_cache)
        return _reference_tuple_inner(x, Wdq, Wuq, Wdkv, Wuk, Wuv, Wo)[0]

    def _L0_ffn_ref(inputs, up_kernel, up_bias, down_kernel, down_bias):
        import jax, jax.numpy as jnp
        import numpy as np
        BLOCK_SIZE = 32
        FP4_GRID = jnp.array([0.0, 0.5, 1.0, 1.5, 2.0, 3.0, 4.0, 6.0], dtype=jnp.float32)
        FP4_MIDS = jnp.array([0.25, 0.75, 1.25, 1.75, 2.5, 3.5, 5.0], dtype=jnp.float32)

        def quantize_to_mxfp4(w, block_size=BLOCK_SIZE):
            K, N = w.shape
            wb = w.reshape(K // block_size, block_size, N)
            amax = jnp.max(jnp.abs(wb), axis=1, keepdims=True)
            exp = jnp.floor(jnp.log2(jnp.maximum(amax, 1e-30))) - 2.0
            scales = jnp.exp2(exp)
            x = wb / scales
            idx = jnp.digitize(jnp.abs(x), FP4_MIDS)
            q = jnp.sign(x) * FP4_GRID[idx]
            return (q, scales)

        def mxfp4_matmul(inputs, q, scales, block_size=BLOCK_SIZE):
            K = inputs.shape[-1]
            N = q.shape[-1]
            w = (q * scales).reshape(K, N)
            return inputs @ w
        q_up, s_up = quantize_to_mxfp4(up_kernel, BLOCK_SIZE)
        x = mxfp4_matmul(inputs, q_up, s_up, BLOCK_SIZE) + up_bias
        x = jax.nn.gelu(x)
        q_dn, s_dn = quantize_to_mxfp4(down_kernel, BLOCK_SIZE)
        x = mxfp4_matmul(x, q_dn, s_dn, BLOCK_SIZE) + down_bias
        return x
    x = L0_attn_x
    x = _layernorm(x + _L0_attn_ref(x, L0_attn_Wdq, L0_attn_Wuq, L0_attn_Wdkv, L0_attn_Wuk, L0_attn_Wuv, L0_attn_Wo), axis=-1)
    x = _layernorm(x + _L0_ffn_ref(x, L0_ffn_up_kernel, L0_ffn_up_bias, L0_ffn_down_kernel, L0_ffn_down_bias), axis=-1)
    return x

_drawn_inputs = setup_inputs


def setup_inputs(seed=0):
    import zlib

    import numpy as np

    out = dict(_drawn_inputs(seed))
    spreads = {'L0_ffn_up_bias': (0.0, 0.1), 'L0_ffn_down_bias': (0.0, 0.1)}
    factors = {'L0_attn_Wdq': 8.0,
     'L0_attn_Wuq': 8.0,
     'L0_attn_Wdkv': 8.0,
     'L0_attn_Wuk': 8.0,
     'L0_attn_Wuv': 8.0,
     'L0_attn_Wo': 8.0}
    for name, (base, spread) in spreads.items():
        noise = np.random.default_rng([zlib.crc32(name.encode()), seed]).standard_normal(out[name].shape)
        drawn = base * np.exp(spread * noise) if base else spread * noise
        out[name] = jnp.asarray(drawn.astype(out[name].dtype))
    for name, factor in factors.items():
        out[name] = (out[name] * factor).astype(out[name].dtype)
    return out
```

```python
from contextlib import ExitStack

import concourse.bass as bass
from concourse import mybir

ALU = mybir.AluOpType
ACT = mybir.ActivationFunctionType
AX_X = mybir.AxisListType.X
F32 = mybir.dt.float32
F32R = mybir.dt.float32r
BF16 = mybir.dt.bfloat16
I32 = mybir.dt.int32

P = 128


class Batch:

    def __init__(self, i, c):
        self.known = c if i is None else None
        self.n = c if i is None else i * 3 + c
        self.m = c % 3
        self.round = c // 3 if i is None else i + c // 3

    def after(self, k):
        return self.known is None or self.known >= k


def mk_layer(nc, x, Wdq, Wuq, Wdkv, Wuk, Wuv, Wo, up_w, up_b, dn_w, dn_b, out):
    NB, T, C = x.shape
    L = Wdkv.shape[0]
    F = up_w.shape[1]
    H = 16
    D = C // H
    NT = NB * T // P
    TB = T // P
    CC = C // P
    HC = P // D
    FC = F // P
    U = 12
    G = 4
    BLK = 32
    NU = NB * T // 512
    NPROD = 6
    MROW = NPROD * D
    ROWS = MROW + 3
    SCALE = float(D) ** -0.5
    EPS = 1e-5
    assert (T, C, L, H, D, F) == (256, 256, 64, 16, 16, 1024)

    K_PARTS = (0, 0, 0, 1, 1, 2)
    Q_PARTS = (0, 1, 2, 0, 1, 0)

    def p1_unit(u):
        g, r = divmod(u, 3)
        return (0, range(G * g, G * g + 4), P) if r == 0 else (1, range(G * g + 2 * r - 2, G * g + 2 * r), T)

    def p2_unit(u):
        g, r = divmod(u, 3)
        return (1, range(G * g, G * g + 4), P) if r == 2 else (0, range(G * g + 2 * r, G * g + 2 * r + 2), T)

    with ExitStack() as top:
        def tile(stack, name, shape, dt):
            return stack.enter_context(nc.sbuf_tensor(name, shape, dt))

        def sem(name):
            return top.enter_context(nc.semaphore(name))

        bank = [top.enter_context(nc.psum_tensor(f"bank{i}", [P, 512], F32)) for i in range(8)]

        resid = tile(top, "resid", [P, NT, C], F32)
        stats = tile(top, "stats", [P, NT, 6], F32)
        w_raw = tile(top, "w_raw", [P, 4096], F32)
        w_q = tile(top, "w_q", [P, 4096], F32R)
        ident = tile(top, "ident", [P, P], F32)
        up_bias = tile(top, "up_bias", [P, FC], F32)
        dn_bias = tile(top, "dn_bias", [P, C], F32)
        wq_up = w_q[:, 0:CC * F].rearrange("p (c f) -> p c f", c=CC)
        wq_dn = w_q[:, CC * F:].rearrange("p (f c) -> p f c", c=C)

        w_loaded = sem("w_loaded")
        ffn_loaded = sem("ffn_loaded")
        const_made = sem("const_made")
        rows_set = sem("rows_set")
        fold_ps = sem("fold_ps")
        fold_sb = sem("fold_sb")
        x_loaded = [sem(f"x_loaded{i}") for i in range(3)]
        xr_loaded = [sem(f"xr_loaded{i}") for i in range(3)]
        stk_loaded = [sem(f"stk_loaded{i}") for i in range(3)]
        nmax_loaded = [sem(f"nmax_loaded{i}") for i in range(3)]
        xT_ready, xT_saved = sem("xT_ready"), sem("xT_saved")
        cc_ready, cc_saved = sem("cc_ready"), sem("cc_saved")
        q_ready, q_hi, q_rest, q_mid, q_lo = (sem(n) for n in ("q_ready", "q_hi", "q_rest", "q_mid", "q_lo"))
        k_ready, k_hi, k_rest, k_mid, k_lo = (sem(n) for n in ("k_ready", "k_hi", "k_rest", "k_mid", "k_lo"))
        v_ready, v_saved = sem("v_ready"), sem("v_saved")
        s1_ready, max_done = sem("s1_ready"), sem("max_done")
        nm_split, nmT_ready, nmT_saved = sem("nm_split"), sem("nmT_ready"), sem("nmT_saved")
        s2_ready, exp_done = sem("s2_ready"), sem("exp_done")
        pv_ready, yT_saved = sem("pv_ready"), sem("yT_saved")
        y_ready, rs_done, yn_done, resid_done, stats_done = (
            sem(n) for n in ("y_ready", "rs_done", "yn_done", "resid_done", "stats_done"))
        quant, quant_end = sem("quant"), sem("quant_end")
        rstd_chain = sem("rstd_chain")

        ln1_mean = tile(top, "ln1_mean", [P, NT], F32)
        ln1_rstd = tile(top, "ln1_rstd", [P, NT], F32)
        newton_a = tile(top, "newton_a", [P, NT], F32)
        newton_v = tile(top, "newton_v", [P, NT], F32)

        LN_STEPS = 17

        def layernorm_steps(chain, count, st, mean, rstd, v, a):
            dve = nc.vector

            def link(ins):
                nonlocal count
                count = count + 1
                ins.then_inc(chain, 1)
                dve.wait_ge(chain, count)

            link(dve.tensor_tensor(a, st[:, :, 1], st[:, :, 4], ALU.subtract))
            link(dve.scalar_tensor_tensor(a, a, 0.25, a, ALU.mult, ALU.mult))
            link(dve.tensor_tensor(v, st[:, :, 2], st[:, :, 5], ALU.add))
            link(dve.scalar_tensor_tensor(v, v, 1.0 / C, a, ALU.mult, ALU.add))
            link(dve.tensor_scalar(v, v, EPS, None, ALU.add))
            link(dve.tensor_tensor(mean, st[:, :, 1], st[:, :, 4], ALU.add))
            link(dve.tensor_scalar(mean, mean, 0.5, None, ALU.mult))
            link(dve.tensor_scalar(rstd.bitcast(I32), v.bitcast(I32), -0.5, 1597463007.0, ALU.mult, ALU.add))
            for _ in range(3):
                link(dve.scalar_tensor_tensor(a, rstd, -0.5, rstd, ALU.mult, ALU.mult))
                link(dve.tensor_tensor(a, a, v, ALU.mult))
                link(dve.scalar_tensor_tensor(rstd, a, 1.5, rstd, ALU.add, ALU.mult))

        with ExitStack() as pa:
            ident_bf = tile(pa, "ident_bf", [P, P], BF16)
            mask_qk = tile(pa, "mask_qk", [P, 4, P], BF16)
            mask_kq = tile(pa, "mask_kq", [P, 4, P], BF16)
            wd = tile(pa, "wd", [P, C], F32)
            wuqP = tile(pa, "wuqP", [P, CC, P], F32)
            wukP = tile(pa, "wukP", [P, CC, P], F32)
            wuvP = tile(pa, "wuvP", [P, CC, P], F32)
            wo = tile(pa, "wo", [P, CC, C], F32)
            up_b_rows = tile(pa, "up_b_rows", [FC, P], F32)
            wdT = tile(pa, "wdT", [P, CC, P], F32)
            wuqT = tile(pa, "wuqT", [P, C], F32)
            wqT = tile(pa, "wqT", [P, CC, D, HC], F32)
            wkT = tile(pa, "wkT", [P, CC, D, HC], F32)
            foldT = tile(pa, "foldT", [P, CC, C], F32)
            woT = tile(pa, "woT", [P, CC, C], F32)
            wv = tile(pa, "wv", [P, C], F32)

            x_in = [tile(pa, f"x_in{i}", [P, TB, C], F32) for i in range(3)]
            xr = [tile(pa, f"xr{i}", [P, TB, C], F32) for i in range(3)]
            xT = tile(pa, "xT", [P, CC, T], F32)
            ccT = tile(pa, "ccT", [P, T], F32)
            qp = [tile(pa, f"q_part{i}", [P, CC, T], BF16) for i in range(3)]
            kp = [tile(pa, f"k_part{i}", [P, CC, T], BF16) for i in range(3)]
            q_r = tile(pa, "q_r", [P, CC, T], F32)
            k_r = tile(pa, "k_r", [P, CC, T], F32)
            q_stk = [tile(pa, f"q_stk{i}", [P, H, T], BF16) for i in range(3)]
            k_stk = [tile(pa, f"k_stk{i}", [P, H, T], BF16) for i in range(3)]
            v_sb = [tile(pa, f"v_sb{i}", [P, TB, H, BLK], F32) for i in range(3)]
            nmax = tile(pa, "nmax", [P, TB, H], F32)
            nmax_r = tile(pa, "nmax_r", [P, TB, H], F32)
            nm_part = tile(pa, "nm_part", [P, TB, 8, H], BF16)
            nmT = tile(pa, "nmT", [3 * H, T], BF16)
            p0 = tile(pa, "p0", [P, H, T], F32)
            p1 = tile(pa, "p1", [P, H, P], F32)
            yT = [tile(pa, f"yT{i}", [P, 2, T], F32) for i in range(2)]
            rs = tile(pa, "rs", [P, TB, H], F32)
            yn = tile(pa, "yn", [P, TB, C], F32)
            qt_w = tile(pa, "qt_w", [P, 256], F32)
            qt_s = tile(pa, "qt_s", [P, 8], F32)
            qt_i = tile(pa, "qt_i", [P, 8], F32)
            qt_x = tile(pa, "qt_x", [P, 256], F32)
            qt_m = tile(pa, "qt_m", [P, 256], F32)
            qt_y = tile(pa, "qt_y", [P, 256], F32)

            PS1, PS2, PROJ = bank[0:2], bank[2:4], bank[4:6]
            PV, SIDE = bank[6], bank[7]

            x_v = x.rearrange("b (t p) c -> p (b t) c", p=P)

            with nc.Block() as block:

                @block.sync
                def _(sp):
                    sp.dma_start(wd[0:L, :], Wdq).then_inc(w_loaded, 16)
                    sp.dma_start(wd[L:2 * L, :], Wdkv).then_inc(w_loaded, 16)
                    sp.dma_start(wuqP[:, :, 0:L], Wuq.rearrange("(c p) l -> p c l", p=P)).then_inc(w_loaded, 16)
                    sp.dma_start(x_in[0][:], x_v[:, 0:TB, :]).then_inc(x_loaded[0], 16)
                    sp.dma_start(wukP[:, :, L:2 * L], Wuk.rearrange("(c p) l -> p c l", p=P)).then_inc(w_loaded, 16)
                    sp.dma_start(wuvP[:, :, L:2 * L], Wuv.rearrange("(c p) l -> p c l", p=P)).then_inc(w_loaded, 16)
                    sp.dma_start(wo[:], Wo.rearrange("(c p) m -> p c m", p=P)).then_inc(w_loaded, 16)
                    sp.dma_start(up_b_rows[:], up_b.rearrange("(f p) -> f p", p=P)).then_inc(w_loaded, 16)
                    sp.dma_start(x_in[1][:], x_v[:, TB:2 * TB, :]).then_inc(x_loaded[1], 16)
                    sp.dma_start(w_raw[:, 0:CC * F], up_w.rearrange("(c p) f -> p c f", p=P)).then_inc(ffn_loaded, 16)
                    sp.dma_start(w_raw[:, CC * F:], dn_w.rearrange("(f p) c -> p f c", p=P)).then_inc(ffn_loaded, 16)
                    sp.dma_start(dn_bias[:], dn_b.partition_broadcast(P)).then_inc(ffn_loaded, 16)

                    def live(i, c):
                        return i is not None or 0 <= c < NB

                    def step(i, s):
                        if live(i, s + 3) and not (i is None and s + 3 < 2):
                            b = Batch(i, s + 3)
                            if b.after(3):
                                sp.wait_ge(xT_ready, b.n - 2)
                            sp.dma_start(x_in[b.m][:], x_v[:, bass.ds(b.n * TB, TB), :]).then_inc(x_loaded[b.m], 16)
                        if live(i, s):
                            b = Batch(i, s)
                            if b.after(3):
                                sp.wait_ge(resid_done, (b.n - 2) * TB)
                            sp.dma_start(xr[b.m][:], x_v[:, bass.ds(b.n * TB, TB), :]).then_inc(xr_loaded[b.m], 16)
                            sp.wait_ge(nmT_saved, b.n + 1)
                            sp.dma_start(q_stk[b.m][MROW:ROWS, :, :], nmT[:, :]).then_inc(nmax_loaded[b.m], 16)
                        if live(i, s + 2):
                            b = Batch(i, s + 2)
                            if b.after(3):
                                sp.wait_ge(s2_ready, (b.n - 2) * U)
                            for part, (qs, ks) in enumerate(((q_hi, k_hi), (q_mid, k_mid), (q_lo, k_lo))):
                                for done, names, parts, stk in ((qs, Q_PARTS, qp, q_stk), (ks, K_PARTS, kp, k_stk)):
                                    sp.wait_ge(done, b.n + 1)
                                    for r in range(NPROD):
                                        if names[r] == part:
                                            sp.dma_start(
                                                stk[b.m][r * D:(r + 1) * D, :, :].rearrange("d (h c) t -> d h (c t)", c=CC),
                                                parts[part][:, :, :].rearrange("p c t -> p (c t)")).then_inc(stk_loaded[b.m], 16)

                    for s in range(-2, 4):
                        step(None, s)
                    with sp.Fori(0, 3) as i:
                        for s in range(4, 7):
                            step(i, s)
                    for s in range(13, 17):
                        step(None, s)

                @block.tensor
                def _(pe):
                    def mm(o, lhsT, rhs, start=True, stop=True, **kw):
                        return nc.tensor.matmul(o, lhsT, rhs, start=start, stop=stop, **kw)

                    pe.wait_ge(const_made, 6)
                    pe.wait_ge(w_loaded, 7 * 16)
                    for c in range(CC):
                        nc.tensor.transpose(bank[0][:, c * P:(c + 1) * P], wd[:, c * P:(c + 1) * P], ident[:])
                    last = nc.tensor.transpose(bank[0][:, C:C + FC], up_b_rows[:], ident[0:FC, 0:FC])
                    last.then_inc(fold_ps, 1)
                    for c in range(CC):
                        last = nc.tensor.transpose(bank[1][:, c * P:(c + 1) * P], wuqP[:, c, :], ident[:])
                    last.then_inc(fold_ps, 1)
                    for j in range(CC):
                        for m in range(CC):
                            last = nc.tensor.transpose(bank[2][:, m * C + j * P:m * C + (j + 1) * P],
                                                       wo[:, j, m * P:(m + 1) * P], ident[:])
                    last.then_inc(fold_ps, 1)
                    pe.wait_ge(fold_sb, 2)
                    for m in range(CC):
                        last = mm(bank[3][:, m * C:(m + 1) * C], wuqT[0:L, m * P:(m + 1) * P], wd[0:L, :])
                    last.then_inc(fold_ps, 1)
                    pe.wait_ge(fold_sb, 5)
                    for m in range(CC):
                        last = mm(bank[4][:, 0:C], wuvP[:, m, :], woT[:, m, :], start=m == 0, stop=m == CC - 1)
                    last.then_inc(fold_ps, 1)
                    pe.wait_ge(fold_sb, 6)
                    for m in range(CC):
                        last = mm(bank[5][:, 0:C], wukP[:, m, :], foldT[:, m, :], start=m == 0, stop=m == CC - 1)
                    last.then_inc(fold_ps, 1)
                    pe.wait_ge(fold_sb, 9)
                    pe.wait_ge(rows_set, 15)

                    def live(i, c):
                        return i is not None or 0 <= c < NB

                    def first_scores(b, u):
                        if u == 0:
                            pe.wait_ge(stk_loaded[b.m], (b.round + 1) * (16 * 2 * NPROD))
                        if u >= 2 or b.after(1):
                            pe.wait_ge(max_done, b.n * U + (u - 1))
                        qb, heads, keys = p1_unit(u)
                        ps = PS1[u % 2][:, :].rearrange("p (h k) -> p h k", k=keys)
                        n = len(heads)
                        mm(ps[:, :, keys - P:keys], ident_bf[:], mask_qk[:, 0:n, :], stop=False, skip_group_check=True)
                        for j, h in enumerate(heads):
                            last = mm(ps[:, j, :], q_stk[b.m][0:MROW, h, qb * P:(qb + 1) * P],
                                      k_stk[b.m][0:MROW, h, 0:keys], start=False, stop=j == n - 1, skip_group_check=True)
                        last.then_inc(s1_ready, 1)

                    def second_scores(b, u):
                        if u == 0:
                            pe.wait_ge(nmax_loaded[b.m], (b.round + 1) * 16)
                        if u >= 2 or b.after(1):
                            pe.wait_ge(exp_done, b.n * U + (u - 1))
                        kb, heads, queries = p2_unit(u)
                        ps = PS2[u % 2][:, :].rearrange("p (h q) -> p h q", q=queries)
                        n = len(heads)
                        mm(ps[:, :, 0:P], ident_bf[:], mask_kq[:, 0:n, :], stop=False, skip_group_check=True)
                        for j, h in enumerate(heads):
                            last = mm(ps[:, j, :], k_stk[b.m][0:ROWS, h, kb * P:(kb + 1) * P],
                                      q_stk[b.m][0:ROWS, h, T - queries:T], start=False, stop=j == n - 1,
                                      skip_group_check=True)
                        last.then_inc(s2_ready, 1)

                    def v_product(b):
                        pe.wait_ge(cc_saved, b.n + 1)
                        pe.wait_ge(k_rest, b.n + 1)
                        for t in range(TB):
                            last = mm(PROJ[0][:, t * C:(t + 1) * C], ccT[:, t * P:(t + 1) * P], wv[:])
                        last.then_inc(v_ready, 1)

                    def x_transposes(b):
                        pe.wait_ge(x_loaded[b.m], (b.round + 1) * 16)
                        if b.after(4):
                            pe.wait_ge(yn_done, (b.n - 3) * TB)
                        if b.after(1):
                            pe.wait_ge(q_rest, b.n)
                        for c in range(CC):
                            for t in range(TB):
                                last = nc.tensor.transpose(PROJ[1][:, c * T + t * P:c * T + (t + 1) * P],
                                                           x_in[b.m][:, t, c * P:(c + 1) * P], ident[:])
                        last.then_inc(xT_ready, 1)

                    def down_projection(b):
                        pe.wait_ge(xT_saved, b.n + 1)
                        if b.after(1):
                            pe.wait_ge(v_saved, b.n)
                        for c in range(CC):
                            last = mm(PROJ[0][:, 0:T], wdT[:, c, :], xT[:, c, :], start=c == 0, stop=c == CC - 1)
                        last.then_inc(cc_ready, 1)

                    def projection(b, w, ps, ready):
                        pe.wait_ge(cc_saved, b.n + 1)
                        for c in range(CC):
                            last = mm(ps[:, c * T:(c + 1) * T], w[:, c, :, :], ccT[:])
                        last.then_inc(ready, 1)

                    def nmax_transposes(b):
                        pe.wait_ge(nm_split, (b.n + 1) * 4)
                        if b.after(2):
                            pe.wait_ge(yn_done, (b.n - 2) * TB + 1)
                        elif b.after(1):
                            pe.wait_ge(nmT_saved, b.n)
                        for t in range(TB):
                            last = nc.tensor.transpose(SIDE[:, :].bitcast(BF16)[:, t * P:(t + 1) * P],
                                                       nm_part[:, t, :, :], ident_bf[:])
                        last.then_inc(nmT_ready, 1)

                    def values(b, g):
                        pe.wait_ge(exp_done, b.n * U + (3 * g + 3))
                        if g == 0:
                            pe.wait_ge(v_saved, b.n + 1)
                        if g % 2 == 0 and (b.after(1) or g == 2):
                            pe.wait_ge(yT_saved, b.n * 2 + g // 2)
                        cols = (g % 2) * T
                        for j in range(G):
                            h = G * g + j
                            mm(PV[BLK * j:BLK * (j + 1), cols:cols + T], v_sb[b.m][:, 0, h, :], p0[:, h, :],
                               stop=False, skip_group_check=True)
                        for j in range(G):
                            h = G * g + j
                            last = mm(PV[BLK * j:BLK * (j + 1), cols + P:cols + T], v_sb[b.m][:, 1, h, :], p1[:, h, :],
                                      start=False, skip_group_check=True)
                        last.then_inc(pv_ready, 1)

                    def y_transposes(b, t):
                        ps = SIDE if t == 0 else PROJ[1]
                        if t == 0:
                            pe.wait_ge(yT_saved, (b.n + 1) * 2)
                            if b.known is None or b.known + 1 < NB:
                                pe.wait_ge(nmT_saved, b.n + 2)
                            else:
                                pe.wait_ge(yn_done, b.n * TB - 1)
                        elif b.known is None or b.known + 3 < NB:
                            pe.wait_ge(q_rest, b.n + 4)
                        else:
                            pe.wait_ge(yn_done, b.n * TB)
                        for g in range(G):
                            last = nc.tensor.transpose(ps[:, g * P:(g + 1) * P],
                                                       yT[g // 2][:, g % 2, t * P:(t + 1) * P], ident[:])
                        last.then_inc(y_ready, 1)

                    def step(i, s):
                        old, now, nxt, far = (Batch(i, s + k) for k in (-1, 0, 1, 2))
                        has_old, has_now, has_nxt, has_far = (live(i, s + k) for k in (-1, 0, 1, 2))
                        for u in range(U):
                            if has_nxt:
                                first_scores(nxt, u)
                            if u < 6 and has_old:
                                second_scores(old, u + 6)
                            if u >= 6 and has_now:
                                second_scores(now, u - 6)
                            if u == 0 and has_nxt:
                                v_product(nxt)
                            if u == 1 and has_now:
                                nmax_transposes(now)
                            if u == 1 and has_far:
                                x_transposes(far)
                            if u == 2 and has_old:
                                values(old, 1)
                            if u == 3 and has_far:
                                down_projection(far)
                            if u == 4 and has_far:
                                projection(far, wqT, PROJ[1], q_ready)
                            if u == 5 and has_old:
                                values(old, 2)
                            if u == 6 and has_far:
                                projection(far, wkT, PROJ[0], k_ready)
                            if u == 8 and has_old:
                                values(old, 3)
                            if u == 9 and has_old:
                                y_transposes(old, 0)
                            if u == 10 and has_old:
                                y_transposes(old, 1)
                            if u == 11 and has_now:
                                values(now, 0)

                    for s in range(-2, 4):
                        step(None, s)
                    with pe.Fori(0, 3) as i:
                        for s in range(4, 7):
                            step(i, s)
                    for s in range(13, 17):
                        step(None, s)

                @block.scalar
                def _(act):
                    def live(i, c):
                        return i is not None or 0 <= c < NB

                    def exponentials(b, u):
                        act.wait_ge(s2_ready, b.n * U + (u + 1))
                        kb, heads, queries = p2_unit(u)
                        g = u // 3
                        if u % 3 == 0 and b.after(1):
                            act.wait_ge(pv_ready, b.n * G + (g - 3))
                        h0, n = heads[0], len(heads)
                        dst = (p1 if kb else p0)[:, h0:h0 + n, :]
                        nc.scalar.activation(dst, PS2[u % 2][:, :].rearrange("p (h q) -> p h q", h=n), ACT.Exp,
                                             scale=SCALE).then_inc(exp_done, 1)

                    def save_v(b):
                        act.wait_ge(v_ready, b.n + 1)
                        nc.scalar.activation(v_sb[b.m][:, :, :, 0:D],
                                             PROJ[0][:, :].rearrange("p (t h d) -> p t h d", t=TB, h=H),
                                             ACT.Copy).then_inc(v_saved, 1)

                    def save_nmT(b):
                        act.wait_ge(nmT_ready, b.n + 1)
                        if b.after(1):
                            act.wait_ge(nmax_loaded[(b.m + 2) % 3], (b.round if b.m == 0 else b.round + 1) * 16)
                        nc.scalar.activation(nmT[:, :], SIDE[:, :].bitcast(BF16)[0:3 * H, 0:T],
                                             ACT.Copy).then_inc(nmT_saved, 1)

                    def save_xT(b):
                        act.wait_ge(xT_ready, b.n + 1)
                        if b.after(1):
                            act.wait_ge(cc_ready, b.n)
                        nc.scalar.activation(xT[:, :, :], PROJ[1][:, :].rearrange("p (c t) -> p c t", c=CC),
                                             ACT.Copy).then_inc(xT_saved, 1)

                    def save_cc(b):
                        act.wait_ge(cc_ready, b.n + 1)
                        if b.after(1):
                            act.wait_ge(v_ready, b.n)
                        nc.scalar.activation(ccT[:, :], PROJ[0][:, 0:T], ACT.Copy).then_inc(cc_saved, 1)

                    def save_yT(b, half):
                        act.wait_ge(pv_ready, b.n * G + 2 * (half + 1))
                        if b.after(1):
                            act.wait_ge(y_ready, b.n * TB)
                        nc.scalar.activation(yT[half][:, :, :], PV[:, :].rearrange("p (g q) -> p g q", g=2),
                                             ACT.Copy).then_inc(yT_saved, 1)

                    def hi_part(b, ps, ready, part, done):
                        act.wait_ge(ready, b.n + 1)
                        if b.after(1):
                            act.wait_ge(stk_loaded[(b.m + 2) % 3],
                                        (b.round if b.m == 0 else b.round + 1) * (16 * 2 * NPROD))
                        nc.scalar.activation(part[:, :, :], ps[:, :].rearrange("p (c t) -> p c t", c=CC),
                                             ACT.Copy).then_inc(done, 1)

                    def mid_part(b, rest, rest_done, part, done):
                        act.wait_ge(rest_done, b.n + 1)
                        nc.scalar.activation(part[:, :, :], rest[:, :, :], ACT.Copy).then_inc(done, 1)

                    def step(i, s):
                        old, now, nxt, far = (Batch(i, s + k) for k in (-1, 0, 1, 2))
                        has_old, has_now, has_nxt, has_far = (live(i, s + k) for k in (-1, 0, 1, 2))
                        for u in range(U):
                            if u < 6 and has_old:
                                exponentials(old, u + 6)
                            if u >= 6 and has_now:
                                exponentials(now, u - 6)
                            if u == 0 and has_nxt:
                                save_v(nxt)
                            if u == 1 and has_now:
                                save_nmT(now)
                            if u == 1 and has_far:
                                save_xT(far)
                            if u == 2 and has_old:
                                save_yT(old, 0)
                            if u == 3 and has_far:
                                save_cc(far)
                            if u == 4 and has_far:
                                hi_part(far, PROJ[1], q_ready, qp[0], q_hi)
                            if u == 6 and has_far:
                                mid_part(far, q_r, q_rest, qp[1], q_mid)
                                hi_part(far, PROJ[0], k_ready, kp[0], k_hi)
                            if u == 8 and has_far:
                                mid_part(far, k_r, k_rest, kp[1], k_mid)
                            if u == 8 and has_old:
                                save_yT(old, 1)

                    for s in range(-2, 4):
                        step(None, s)
                    with act.Fori(0, 3) as i:
                        for s in range(4, 7):
                            step(i, s)
                    for s in range(13, 17):
                        step(None, s)

                @block.gpsimd
                def _(pool):
                    pool.memset(ident[:], 0.0).then_inc(rows_set, 1)
                    pool.memset(ident_bf[:], 0.0).then_inc(rows_set, 1)
                    pool.memset(mask_qk[:], 0.0).then_inc(rows_set, 1)
                    pool.memset(mask_kq[:], 0.0).then_inc(rows_set, 1)
                    pool.wait_ge(rows_set, 4)
                    for t in (ident, ident_bf):
                        pool.affine_select(out=t[:], in_=t[:], compare_op=ALU.not_equal, fill=1.0, base=0,
                                           pattern=[[-1, P]], channel_multiplier=1).then_inc(const_made, 1)
                    for t, sign in ((mask_qk, 1), (mask_kq, -1)):
                        pool.affine_select(out=t[:], in_=t[:], compare_op=ALU.is_ge, fill=-3.0e38, base=0,
                                           pattern=[[0, 4], [-sign, P]], channel_multiplier=sign).then_inc(rows_set, 1)
                    for t in range(3):
                        pool.wait_ge(rows_set, 6 + t)
                        pool.memset(k_stk[t][MROW:ROWS, :, :], 1.0).then_inc(rows_set, 1)
                    pool.wait_ge(rows_set, 9)
                    for t in range(3):
                        pool.memset(v_sb[t][:, :, :, D:D + 1], 1.0).then_inc(rows_set, 1)
                        pool.memset(v_sb[t][:, :, :, D + 1:BLK], 0.0).then_inc(rows_set, 1)

                    def live(i, c):
                        return i is not None or 0 <= c < NB

                    def lo_part(b, rest, mid, mid_done, part, done):
                        pool.wait_ge(mid_done, b.n + 1)
                        pool.tensor_tensor(part[:, :, :], rest[:, :, :], mid[:, :, :], ALU.subtract).then_inc(done, 1)

                    def residual(b, t):
                        pool.wait_ge(yn_done, b.n * TB + (t + 1))
                        if t == 0:
                            pool.wait_ge(xr_loaded[b.m], (b.round + 1) * 16)
                        pool.tensor_tensor(resid[:, bass.ds(b.n * TB + t, 1), :], yn[:, t:t + 1, :],
                                           xr[b.m][:, t:t + 1, :], ALU.add).then_inc(resid_done, 1)

                    def step(i, s):
                        old, far = (Batch(i, s + k) for k in (-1, 2))
                        has_old, has_far = (live(i, s + k) for k in (-1, 2))
                        if has_far:
                            lo_part(far, q_r, qp[1], q_mid, qp[2], q_lo)
                            lo_part(far, k_r, kp[1], k_mid, kp[2], k_lo)
                        if has_old:
                            for t in range(TB):
                                residual(old, t)

                    for s in range(-2, 4):
                        step(None, s)
                    with pool.Fori(0, 3) as i:
                        for s in range(4, 7):
                            step(i, s)
                    for s in range(13, 17):
                        step(None, s)

                @block.vector
                def _(dve):
                    for t in (wuqP, wukP, wuvP):
                        half = t[:, :, L:2 * L] if t is wuqP else t[:, :, 0:L]
                        nc.vector.memset(half, 0.0).then_inc(const_made, 1)
                    nc.vector.memset(nm_part[:], 0.0).then_inc(const_made, 1)

                    def copy(dst, src, n):
                        dve.wait_ge(fold_ps, n)
                        nc.vector.tensor_copy(dst, src).then_inc(fold_sb, 1)

                    def heads_inner(t):
                        return t.rearrange("p (c h d) -> p c d h", c=CC, h=HC)

                    copy(wdT[:], bank[0][:, 0:C].rearrange("p (c l) -> p c l", c=CC), 1)
                    nc.vector.tensor_copy(up_bias[:], bank[0][:, C:C + FC])
                    copy(wuqT[:], bank[1][:, 0:C], 2)
                    for c in range(CC):
                        nc.vector.tensor_copy(wqT[:, c], heads_inner(bank[1][:, 0:C])[:, c]).then_inc(fold_sb, 1)
                    copy(woT[:], bank[2][:, :].rearrange("p (c j) -> p c j", c=CC), 3)
                    copy(foldT[:], bank[3][:, :].rearrange("p (c j) -> p c j", c=CC), 4)
                    copy(wv[:].rearrange("p (h c d) -> p c h d", h=HC, c=CC),
                         bank[4][:, 0:C].rearrange("p (c h d) -> p c h d", c=CC, h=HC), 5)
                    dve.wait_ge(fold_ps, 6)
                    for c in range(CC):
                        nc.vector.tensor_copy(wkT[:, c], heads_inner(bank[5][:, 0:C])[:, c]).then_inc(fold_sb, 1)

                    def live(i, c):
                        return i is not None or 0 <= c < NB

                    def maxima(b, u):
                        dve.wait_ge(s1_ready, b.n * U + (u + 1))
                        qb, heads, keys = p1_unit(u)
                        h0, n = heads[0], len(heads)
                        nc.vector.tensor_reduce(nmax[:, qb, h0:h0 + n], PS1[u % 2][:, :].rearrange("p (h k) -> p h k", h=n),
                                                axis=AX_X, op=ALU.max, negate=True).then_inc(max_done, 1)

                    def split_nmax(b):
                        n0 = b.n * 4
                        dve.wait_ge(max_done, (b.n + 1) * U)
                        if b.after(1):
                            dve.wait_ge(nmT_ready, b.n)
                        nc.vector.tensor_copy(nm_part[:, :, 0, :], nmax[:]).then_inc(nm_split, 1)
                        dve.wait_ge(nm_split, n0 + 1)
                        nc.vector.tensor_tensor(nmax_r[:], nmax[:], nm_part[:, :, 0, :], ALU.subtract).then_inc(nm_split, 1)
                        dve.wait_ge(nm_split, n0 + 2)
                        nc.vector.tensor_copy(nm_part[:, :, 1, :], nmax_r[:]).then_inc(nm_split, 1)
                        dve.wait_ge(nm_split, n0 + 3)
                        nc.vector.tensor_tensor(nm_part[:, :, 2, :], nmax_r[:], nm_part[:, :, 1, :],
                                                ALU.subtract).then_inc(nm_split, 1)

                    def rest_part(b, ps, hi, hi_done, lo_done, rest, done):
                        dve.wait_ge(hi_done, b.n + 1)
                        if b.after(1):
                            dve.wait_ge(lo_done, b.n)
                        nc.vector.tensor_tensor(rest[:, :, :], ps[:, :].rearrange("p (c t) -> p c t", c=CC), hi[:, :, :],
                                                ALU.subtract).then_inc(done, 1)

                    def normalise(b, t):
                        n = b.n * TB + t
                        ps = (SIDE if t == 0 else PROJ[1])[:, :].rearrange("p (h e) -> p h e", e=BLK)
                        dve.wait_ge(y_ready, n + 1)
                        nc.vector.reciprocal(rs[:, t, :], ps[:, :, D]).then_inc(rs_done, 1)
                        dve.wait_ge(rs_done, n + 1)
                        if b.after(1):
                            dve.wait_ge(resid_done, n - 1)
                        nc.vector.tensor_tensor(
                            yn[:, t, :].rearrange("p (c h d) -> p h c d", c=CC, h=HC),
                            ps[:, :, 0:D].rearrange("p (h c) d -> p h c d", c=CC),
                            rs[:, t, :].rearrange("p (h c) -> p h c", c=CC).unsqueeze(3).to_broadcast([P, HC, CC, D]),
                            ALU.mult).then_inc(yn_done, 1)

                    def statistics(b, t):
                        n = b.n * TB + t
                        dve.wait_ge(resid_done, n + 1)
                        nc.vector.bn_stats(stats[:, bass.ds(n, 1), :].rearrange("p a s -> p (a s)"),
                                           resid[:, bass.ds(n, 1), :].rearrange("p a c -> p (a c)")).then_inc(stats_done, 1)

                    QSTEPS = 13

                    def quantise(n):
                        w = w_raw[:, bass.ds(n * 256, 256)]
                        count = n * QSTEPS

                        def link(ins):
                            nonlocal count
                            count = count + 1
                            ins.then_inc(quant, 1)
                            dve.wait_ge(quant, count)

                        def blocks(t):
                            return t[:].rearrange("p (j k) -> p j k", k=BLK)

                        def per_block(t):
                            return t[:].unsqueeze(2).to_broadcast([P, 8, BLK])

                        link(nc.vector.tensor_copy(qt_x[:], w))
                        link(nc.vector.transpose(qt_w[:], qt_x[:]))
                        link(nc.vector.tensor_reduce(qt_s[:], blocks(qt_w), axis=AX_X, op=ALU.max,
                                                     apply_absolute_value=True))
                        link(nc.vector.tensor_scalar(qt_s[:], qt_s[:], 1e-30, None, ALU.max))
                        link(nc.vector.tensor_scalar(qt_s[:].bitcast(I32), qt_s[:].bitcast(I32), 0x7F800000, None,
                                                     ALU.bitwise_and))
                        link(nc.vector.tensor_scalar(qt_s[:], qt_s[:], 0.25, None, ALU.mult))
                        link(nc.vector.tensor_scalar(qt_i[:].bitcast(I32), qt_s[:].bitcast(I32), -1.0, float(254 << 23),
                                                     ALU.mult, ALU.add))
                        link(nc.vector.tensor_tensor(blocks(qt_x), blocks(qt_w), per_block(qt_i), ALU.mult))
                        link(nc.vector.tensor_scalar(qt_y[:].bitcast(I32), qt_x[:].bitcast(I32), 0x7FE00000, None,
                                                     ALU.bitwise_and))
                        link(nc.vector.tensor_scalar(qt_m[:].bitcast(I32), qt_x[:].bitcast(I32), 0x7F800000, None,
                                                     ALU.bitwise_and))
                        link(nc.vector.tensor_scalar(qt_m[:], qt_m[:], 1.0, 1.5 * 2.0 ** 22, ALU.max, ALU.mult))
                        link(nc.vector.scalar_tensor_tensor(qt_y[:], qt_y[:], 1.0 + 2.0 ** -6, qt_m[:], ALU.mult, ALU.add))
                        link(nc.vector.tensor_tensor(qt_y[:], qt_y[:], qt_m[:], ALU.subtract))

                    QTAIL = 4

                    def quantise_end(n):
                        count = n * QTAIL

                        def link(ins):
                            nonlocal count
                            count = count + 1
                            ins.then_inc(quant_end, 1)
                            dve.wait_ge(quant_end, count)

                        link(nc.vector.scalar_tensor_tensor(qt_m[:].rearrange("p (j k) -> p j k", k=BLK),
                                                            qt_y[:].rearrange("p (j k) -> p j k", k=BLK), 6.0,
                                                            qt_s[:].unsqueeze(2).to_broadcast([P, 8, BLK]),
                                                            ALU.min, ALU.mult))
                        link(nc.vector.tensor_scalar(qt_x[:].bitcast(I32), qt_w[:].bitcast(I32), -0x80000000, None,
                                                     ALU.bitwise_and))
                        link(nc.vector.tensor_tensor(qt_y[:].bitcast(I32), qt_m[:].bitcast(I32), qt_x[:].bitcast(I32),
                                                     ALU.bitwise_or))
                        link(nc.vector.transpose(qt_m[:], qt_y[:]))
                        nc.vector.tensor_copy(w_q[:, bass.ds(n * 256, 256)], qt_m[:])

                    def step(i, s):
                        older, old, now, nxt, far = (Batch(i, s + k) for k in (-2, -1, 0, 1, 2))
                        has_older, has_old, has_now, has_nxt, has_far = (live(i, s + k) for k in (-2, -1, 0, 1, 2))
                        if s == -2:
                            dve.wait_ge(ffn_loaded, 3 * 16)
                        for u in range(U):
                            if has_nxt:
                                maxima(nxt, u)
                            if u == 1 and has_older:
                                for t in range(TB):
                                    statistics(older, t)
                            if u == 2 and has_now:
                                quantise(now.n)
                            if u == 3 and has_now:
                                quantise_end(now.n)
                            if u == 5 and has_far:
                                rest_part(far, PROJ[1], qp[0], q_hi, q_lo, q_r, q_rest)
                            if u == 7 and has_far:
                                rest_part(far, PROJ[0], kp[0], k_hi, k_lo, k_r, k_rest)
                            if u == 10 and has_old:
                                normalise(old, 0)
                            if u == 11 and has_old:
                                normalise(old, 1)
                        if has_nxt:
                            split_nmax(nxt)

                    for s in range(-2, 4):
                        step(None, s)
                    with dve.Fori(0, 3) as i:
                        for s in range(4, 7):
                            step(i, s)
                    for s in range(13, 18):
                        step(None, s)
                    dve.wait_ge(stats_done, NT)
                    layernorm_steps(rstd_chain, 0, stats, ln1_mean[:], ln1_rstd[:], newton_v[:], newton_a[:])

        with ExitStack() as pb:
            x1 = [tile(pb, f"x1_{i}", [P, 4, C], F32) for i in range(2)]
            x1b = [tile(pb, f"x1b_{i}", [P, 4, C], F32) for i in range(2)]
            x1T_hi = [tile(pb, f"x1T_hi{i}", [P, CC, 512], F32R) for i in range(2)]
            x1T_lo = [tile(pb, f"x1T_lo{i}", [P, CC, 512], F32R) for i in range(2)]
            h_f = [tile(pb, f"h_f{i}", [P, 512], F32) for i in range(4)]
            h_hi = [tile(pb, f"h_hi{i}", [P, 512], F32R) for i in range(4)]
            h_lo = [tile(pb, f"h_lo{i}", [P, 512], F32R) for i in range(4)]
            r2 = [tile(pb, f"r2_{i}", [P, 4, C], F32) for i in range(2)]
            y2 = [tile(pb, f"y2_{i}", [P, 4, C], F32) for i in range(2)]
            st2 = tile(pb, "st2", [P, 4, 6], F32)
            mean2 = tile(pb, "mean2", [P, 4], F32)
            v2 = tile(pb, "v2", [P, 4], F32)
            a2 = tile(pb, "a2", [P, 4], F32)
            rstd2 = tile(pb, "rstd2", [P, 4], F32)

            x1_done, x1b_done = sem("x1_done"), sem("x1b_done")
            x1T_ready, x1T_hi_done, x1T_lo_done = sem("x1T_ready"), sem("x1T_hi_done"), sem("x1T_lo_done")
            up_ready, h_done, h_hi_done, h_lo_done = sem("up_ready"), sem("h_done"), sem("h_hi_done"), sem("h_lo_done")
            dn_step, r2_done, st2_done = sem("dn_step"), sem("r2_done"), sem("st2_done")
            ln2_chain, y2_done, stored = sem("ln2_chain"), sem("y2_done"), [sem("stored0"), sem("stored1")]

            UP, DN, XP = bank[0:2], bank[2:6], bank[6:8]
            LAG = 2

            class Unit:

                def __init__(self, i, c):
                    self.known = c if i is None else None
                    self.n = c if i is None else i * 2 + c
                    self.m = c % 2
                    self.round = c // 2 if i is None else i + c // 2

                def after(self, k):
                    return self.known is None or self.known >= k

            def run(eng, step):
                for s in (-1, 0, 1, 2):
                    step(None, s)
                with eng.Fori(0, (NU - 4) // 2) as i:
                    for s in (3, 4):
                        step(i, s)
                for s in range(NU - 1, NU + 1):
                    step(None, s)

            def live(i, c):
                return i is not None or 0 <= c < NU

            out_v = out.rearrange("b (t p) c -> p (b t) c", p=P)

            with nc.Block() as block:

                @block.sync
                def _(sp):
                    def step(i, s):
                        if live(i, s - 1):
                            b = Unit(i, s - 1)
                            sp.wait_ge(y2_done, (b.n + 1) * 4)
                            sp.dma_start(out_v[:, bass.ds(b.n * 4, 4), :], y2[b.m][:]).then_inc(stored[b.m], 16)

                    run(sp, step)
                    for m in range(2):
                        sp.wait_ge(stored[m], NU // 2 * 16)

                @block.tensor
                def _(pe):
                    def transposes(b, c):
                        pe.wait_ge(x1_done, (b.n + 1) * 4)
                        if b.after(1):
                            pe.wait_ge(x1T_lo_done, b.n * CC + (c - 1))
                        for t in range(4):
                            last = nc.tensor.transpose(XP[c][:, t * P:(t + 1) * P], x1[b.m][:, t, c * P:(c + 1) * P],
                                                       ident[:])
                        last.then_inc(x1T_ready, 1)

                    def up(b, f):
                        if f == 0:
                            pe.wait_ge(x1T_hi_done, (b.n + 1) * CC)
                            pe.wait_ge(x1T_lo_done, (b.n + 1) * CC)
                        if f >= 2 or b.after(1):
                            pe.wait_ge(h_done, b.n * FC + (f - 1))
                        for k, (c, part) in enumerate((c, part) for c in range(CC) for part in (x1T_hi, x1T_lo)):
                            last = nc.tensor.matmul(UP[f % 2][:, :], wq_up[:, c, f * P:(f + 1) * P], part[b.m][:, c, :],
                                                    start=k == 0, stop=k == 3)
                        last.then_inc(up_ready, 1)

                    def down(b, f):
                        pe.wait_ge(h_lo_done, b.n * FC + (f + 1))
                        for t in range(4):
                            if f == 0 and b.after(1):
                                pe.wait_ge(r2_done, b.n * 4 + (t - 3))
                            for part in (h_hi, h_lo):
                                last = nc.tensor.matmul(DN[t][:, 0:C], part[f % 4][:, t * P:(t + 1) * P], wq_dn[:, f, :],
                                                        start=f == 0 and part is h_hi, stop=f == FC - 1 and part is h_lo)
                        last.then_inc(dn_step, 1)

                    def step(i, s):
                        old, now, nxt = (Unit(i, s + k) for k in (-1, 0, 1))
                        for f in range(FC):
                            if live(i, s):
                                up(now, f)
                            if f < LAG and live(i, s - 1):
                                down(old, FC - LAG + f)
                            if f >= LAG and live(i, s):
                                down(now, f - LAG)
                            if f in (3, 4) and live(i, s + 1):
                                transposes(nxt, f - 3)

                    run(pe, step)

                @block.scalar
                def _(act):
                    def gelu(b, f):
                        act.wait_ge(up_ready, b.n * FC + (f + 1))
                        if f >= 4 or b.after(1):
                            act.wait_ge(h_lo_done, b.n * FC + (f - 3))
                        nc.scalar.activation(h_f[f % 4][:], UP[f % 2][:, :], ACT.Gelu_apprx_tanh,
                                             bias=up_bias[:, f:f + 1]).then_inc(h_done, 1)

                    def h_high(b, f):
                        act.wait_ge(h_done, b.n * FC + (f + 1))
                        if f >= 4 or b.after(1):
                            act.wait_ge(dn_step, b.n * FC + (f - 3))
                        nc.scalar.activation(h_hi[f % 4][:], h_f[f % 4][:], ACT.Copy).then_inc(h_hi_done, 1)

                    def x_high(b, c):
                        act.wait_ge(x1T_ready, b.n * CC + (c + 1))
                        if c == 0 and b.after(2):
                            act.wait_ge(up_ready, (b.n - 1) * FC)
                        nc.scalar.activation(x1T_hi[b.m][:, c, :], XP[c][:, :], ACT.Copy).then_inc(x1T_hi_done, 1)

                    def step(i, s):
                        now, nxt = (Unit(i, s + k) for k in (0, 1))
                        for f in range(FC):
                            if live(i, s):
                                gelu(now, f)
                                h_high(now, f)
                            if f in (3, 4) and live(i, s + 1):
                                x_high(nxt, f - 3)

                    run(act, step)

                @block.gpsimd
                def _(pool):
                    def step(i, s):
                        if live(i, s + 1):
                            b = Unit(i, s + 1)
                            pool.wait_ge(x1_done, (b.n + 1) * 4)
                            if b.after(2):
                                pool.wait_ge(r2_done, (b.n - 1) * 4)
                            pool.tensor_tensor(x1b[b.m][:], x1[b.m][:], dn_bias[:].unsqueeze(1).to_broadcast([P, 4, C]),
                                               ALU.add).then_inc(x1b_done, 1)

                    run(pool, step)

                @block.vector
                def _(dve):
                    def layernorm1(b, t):
                        if t == 0 and b.after(2):
                            dve.wait_ge(x1T_ready, (b.n - 1) * CC)
                            dve.wait_ge(x1b_done, b.n - 1)
                        row = b.n * 4 + t
                        nc.vector.tensor_scalar(x1[b.m][:, t:t + 1, :], resid[:, bass.ds(row, 1), :],
                                                ln1_mean[:, bass.ds(row, 1)], ln1_rstd[:, bass.ds(row, 1)],
                                                ALU.subtract, ALU.mult).then_inc(x1_done, 1)

                    def x_low(b, c):
                        dve.wait_ge(x1T_hi_done, b.n * CC + (c + 1))
                        if c == 0 and b.after(2):
                            dve.wait_ge(up_ready, (b.n - 1) * FC)
                        nc.vector.tensor_tensor(x1T_lo[b.m][:, c, :], XP[c][:, :], x1T_hi[b.m][:, c, :].bitcast(F32),
                                                ALU.subtract).then_inc(x1T_lo_done, 1)

                    def h_low(b, f):
                        dve.wait_ge(h_hi_done, b.n * FC + (f + 1))
                        nc.vector.tensor_tensor(h_lo[f % 4][:], h_f[f % 4][:], h_hi[f % 4][:].bitcast(F32),
                                                ALU.subtract).then_inc(h_lo_done, 1)

                    def add_residual(b, t):
                        if t == 0:
                            dve.wait_ge(dn_step, (b.n + 1) * FC)
                            dve.wait_ge(x1b_done, b.n + 1)
                        nc.vector.tensor_tensor(r2[b.m][:, t, :], DN[t][:, 0:C], x1b[b.m][:, t, :],
                                                ALU.add).then_inc(r2_done, 1)

                    def statistics2(b, t):
                        dve.wait_ge(r2_done, b.n * 4 + (t + 1))
                        nc.vector.bn_stats(st2[:, t, :], r2[b.m][:, t, :]).then_inc(st2_done, 1)

                    def rstd_of(b):
                        dve.wait_ge(st2_done, (b.n + 1) * 4)
                        layernorm_steps(ln2_chain, b.n * LN_STEPS, st2, mean2[:], rstd2[:], v2[:], a2[:])

                    def layernorm2(b, t):
                        if t == 0 and b.after(2):
                            dve.wait_ge(stored[b.m], b.round * 16)
                        nc.vector.tensor_scalar(y2[b.m][:, t, :], r2[b.m][:, t, :], mean2[:, t:t + 1], rstd2[:, t:t + 1],
                                                ALU.subtract, ALU.mult).then_inc(y2_done, 1)

                    def step(i, s):
                        old, now, nxt = (Unit(i, s + k) for k in (-1, 0, 1))
                        has_old, has_now, has_nxt = (live(i, s + k) for k in (-1, 0, 1))
                        for f in range(FC):
                            if f == 0 and has_nxt:
                                for t in range(4):
                                    layernorm1(nxt, t)
                            if has_now:
                                h_low(now, f)
                            if f in (3, 4) and has_nxt:
                                x_low(nxt, f - 3)
                            if f == 1 and has_old:
                                for t in range(4):
                                    add_residual(old, t)
                            if f == 2 and has_old:
                                for t in range(4):
                                    statistics2(old, t)
                            if f == 6 and has_old:
                                rstd_of(old)
                            if f == 7 and has_old:
                                for t in range(4):
                                    layernorm2(old, t)

                    run(dve, step)


_INS = ['L0_attn_x', 'L0_attn_Wdq', 'L0_attn_Wuq', 'L0_attn_Wdkv', 'L0_attn_Wuk', 'L0_attn_Wuv', 'L0_attn_Wo',
        'L0_ffn_up_kernel', 'L0_ffn_up_bias', 'L0_ffn_down_kernel', 'L0_ffn_down_bias']
_OUTS = [((16, 256, 256), 'float32')]


def kernel(**inputs):
    import numpy as _np
    import concourse.bacc as _bacc
    from concourse import mybir as _mybir
    from concourse.bass_utils import run_bass_kernel_spmd as _run

    nc = _bacc.Bacc("TRN2", target_bir_lowering=False, num_devices=1)
    arrays, args = {}, []
    for name in _INS:
        a = _np.ascontiguousarray(inputs[name])
        arrays[f"in_{name}_dram"] = a
        args.append(nc.dram_tensor(f"in_{name}_dram", a.shape, _mybir.dt.from_np(a.dtype), kind="ExternalInput").ap())
    for i, (shape, dtype) in enumerate(_OUTS):
        dt = _mybir.dt.from_np(_np.dtype(dtype))
        args.append(nc.dram_tensor(f"out_{i}_dram", shape, dt, kind="ExternalOutput").ap())
    mk_layer(nc, *args)
    r = _run(nc, [arrays], core_ids=[0])
    return r.results[0]["out_0_dram"]
```
